# Optimizing a Trainium2 kernel written in Bass

```python
import numpy as np
import jax
import jax.numpy as jnp

def _softmax(x, axis=-1):
    return jax.nn.softmax(x, axis=axis)

def _gelu(x):
    return jax.nn.gelu(x, approximate=True)

def _silu(x):
    return jax.nn.silu(x)

def _sigmoid(x):
    return jax.nn.sigmoid(x)

def _layernorm(x, axis=-1, eps=1e-05):
    m = jnp.mean(x, axis=axis, keepdims=True)
    v = jnp.var(x, axis=axis, keepdims=True)
    return (x - m) / jnp.sqrt(v + eps)

def _scatter_add(tgt, idx, src, axis=0):
    return tgt.at[idx].add(src)

def _segment_sum(src, seg, n):
    return jax.ops.segment_sum(src, seg, n)
kernel_name = 'mk_cond_seq_d1_seqx_r8_645b6c'

def setup_inputs(seed: int=0):
    np.random.seed(seed)
    _w = jnp.asarray

    def _rec_inputs():
        import jax
        import jax.numpy as jnp
        _rk = jax.random.key(seed)
        x = -0.0002928 + 1 * jax.random.normal(jax.random.fold_in(_rk, 1), (32, 128, 128), jnp.float32)
        _lenS = 128 - jax.random.randint(jax.random.fold_in(_rk, 7), (32,), 0, max(1, 128 // 4) + 1, jnp.int32)
        _lenS2 = 128 - jax.random.randint(jax.random.fold_in(_rk, 8), (32,), 0, max(1, 128 // 4) + 1, jnp.int32)
        fside_BxSxS_0 = -1.39393e-06 + 0.999914 * jax.random.normal(jax.random.fold_in(_rk, 11), (32, 128, 128), jnp.float32)
        cond_1024 = 0.0132156 + 1.00766 * jax.random.normal(jax.random.fold_in(_rk, 12), (32, 128), jnp.float32)
        _validS = jnp.arange(128)[None, :] < _lenS[:, None]
        _validS2 = jnp.arange(128)[None, :] < _lenS2[:, None]
        _causal = jnp.tril(jnp.ones((128, 128), dtype=bool))
        mask_BxS_bk0 = jnp.logical_not(jnp.broadcast_to(_validS[:, :], (32, 128)))
        return (x, fside_BxSxS_0, cond_1024, mask_BxS_bk0)
    x, fside_BxSxS_0, cond_1024, mask_BxS_bk0 = _rec_inputs()

    def _L0_cond_setup():
        import math
        import jax, jax.numpy as jnp
        import numpy as np
        B, S, L = (4, 128, 128)
        D, H = (128, 16)
        HD = D // H
        HIDDEN = 4 * D
        ROPE_BASE = 10000.0
        EPS = 1e-06

        def rmsnorm(x, w):
            return x * jax.lax.rsqrt(jnp.mean(x * x, axis=-1, keepdims=True) + EPS) * w

        def safe_key_padding_mask(mask):
            all_pad = jnp.all(mask, axis=-1, keepdims=True)
            return jnp.where(all_pad, False, mask)

        def split_heads(x):
            b, t, _ = x.shape
            return x.reshape(b, t, H, HD).transpose(0, 2, 1, 3)

        def merge_heads(x):
            b, _, t, _ = x.shape
            return x.transpose(0, 2, 1, 3).reshape(b, t, H * HD)

        def apply_rope(x):
            t = x.shape[-2]
            pos = jnp.arange(t, dtype=jnp.float32)[:, None]
            freqs = jnp.exp(jnp.arange(0, HD, 2, dtype=jnp.float32) * (-math.log(ROPE_BASE) / HD))
            ang = pos * freqs[None, :]
            sin = jnp.sin(ang).astype(x.dtype)
            cos = jnp.cos(ang).astype(x.dtype)
            even, odd = (x[..., 0::2], x[..., 1::2])
            rot = jnp.stack((even * cos - odd * sin, even * sin + odd * cos), axis=-1)
            return rot.reshape(x.shape)

        def masked_attn(q, k, v, valid_keys):
            scores = jnp.einsum('bhqd,bhkd->bhqk', q, k) / math.sqrt(HD)
            scores = jnp.where(valid_keys[:, None, None, :], scores, jnp.finfo(scores.dtype).min)
            return jnp.einsum('bhqk,bhkd->bhqd', jax.nn.softmax(scores, axis=-1), v)
        key = jax.random.key(seed)
        ks = jax.random.split(key, 30)
        sc = 0.02
        n = lambda k, shp: jax.random.normal(k, shp, jnp.float32)
        inp = {'tokens': n(ks[0], (B, S, D)), 'seq_tokens': n(ks[1], (B, L, D)), 'modulation': n(ks[2], (B, D)), 'attn_norm_w': jnp.ones((D,), jnp.float32), 'qkv_w': n(ks[3], (3 * D, D)) * sc, 'qkv_b': jnp.zeros((3 * D,), jnp.float32), 'out_w': n(ks[4], (D, D)) * sc, 'out_b': jnp.zeros((D,), jnp.float32), 'film_w': n(ks[5], (2 * D, D)) * sc, 'film_b': jnp.zeros((2 * D,), jnp.float32), 'sq_norm_w': jnp.ones((D,), jnp.float32), 's_norm_w': jnp.ones((D,), jnp.float32), 'mha_in_w': n(ks[6], (3 * D, D)) * sc, 'mha_in_b': jnp.zeros((3 * D,), jnp.float32), 'mha_out_w': n(ks[7], (D, D)) * sc, 'mha_out_b': jnp.zeros((D,), jnp.float32), 'gate_w': n(ks[8], (D, 2 * D)) * sc, 'gate_b': jnp.zeros((D,), jnp.float32), 'ffn_norm_w': jnp.ones((D,), jnp.float32), 'gu_w': n(ks[9], (2 * HIDDEN, D)) * sc, 'gu_b': jnp.zeros((2 * HIDDEN,), jnp.float32), 'down_w': n(ks[10], (D, HIDDEN)) * sc, 'down_b': jnp.zeros((D,), jnp.float32), 'padding_mask': jax.random.bernoulli(ks[11], 0.1, (B, S)), 'seq_mask': jax.random.bernoulli(ks[12], 0.1, (B, L))}
        return inp
    _L0_cond_all = _L0_cond_setup()
    _L0_cond_in = {k: v for k, v in _L0_cond_all.items() if k in ('attn_norm_w', 'qkv_w', 'qkv_b', 'out_w', 'out_b', 'film_w', 'film_b', 'sq_norm_w', 's_norm_w', 'mha_in_w', 'mha_in_b', 'mha_out_w', 'mha_out_b', 'gate_w', 'gate_b', 'ffn_norm_w', 'gu_w', 'gu_b', 'down_w', 'down_b')}
    del _L0_cond_all
    return {'x': x, 'fside_BxSxS_0': fside_BxSxS_0, 'cond_1024': cond_1024, 'mask_BxS_bk0': mask_BxS_bk0, 'L0_cond_attn_norm_w': _L0_cond_in['attn_norm_w'], 'L0_cond_qkv_w': _L0_cond_in['qkv_w'], 'L0_cond_qkv_b': _L0_cond_in['qkv_b'], 'L0_cond_out_w': _L0_cond_in['out_w'], 'L0_cond_out_b': _L0_cond_in['out_b'], 'L0_cond_film_w': _L0_cond_in['film_w'], 'L0_cond_film_b': _L0_cond_in['film_b'], 'L0_cond_sq_norm_w': _L0_cond_in['sq_norm_w'], 'L0_cond_s_norm_w': _L0_cond_in['s_norm_w'], 'L0_cond_mha_in_w': _L0_cond_in['mha_in_w'], 'L0_cond_mha_in_b': _L0_cond_in['mha_in_b'], 'L0_cond_mha_out_w': _L0_cond_in['mha_out_w'], 'L0_cond_mha_out_b': _L0_cond_in['mha_out_b'], 'L0_cond_gate_w': _L0_cond_in['gate_w'], 'L0_cond_gate_b': _L0_cond_in['gate_b'], 'L0_cond_ffn_norm_w': _L0_cond_in['ffn_norm_w'], 'L0_cond_gu_w': _L0_cond_in['gu_w'], 'L0_cond_gu_b': _L0_cond_in['gu_b'], 'L0_cond_down_w': _L0_cond_in['down_w'], 'L0_cond_down_b': _L0_cond_in['down_b']}

def reference(x, fside_BxSxS_0, cond_1024, mask_BxS_bk0, L0_cond_attn_norm_w, L0_cond_qkv_w, L0_cond_qkv_b, L0_cond_out_w, L0_cond_out_b, L0_cond_film_w, L0_cond_film_b, L0_cond_sq_norm_w, L0_cond_s_norm_w, L0_cond_mha_in_w, L0_cond_mha_in_b, L0_cond_mha_out_w, L0_cond_mha_out_b, L0_cond_gate_w, L0_cond_gate_b, L0_cond_ffn_norm_w, L0_cond_gu_w, L0_cond_gu_b, L0_cond_down_w, L0_cond_down_b):
    import jax
    import jax.numpy as jnp

    def _L0_cond_ref(tokens, seq_tokens, modulation, attn_norm_w, qkv_w, qkv_b, out_w, out_b, film_w, film_b, sq_norm_w, s_norm_w, mha_in_w, mha_in_b, mha_out_w, mha_out_b, gate_w, gate_b, ffn_norm_w, gu_w, gu_b, down_w, down_b, padding_mask, seq_mask):
        import math
        import jax, jax.numpy as jnp
        import numpy as np
        B, S, L = (4, 128, 128)
        D, H = (128, 16)
        HD = D // H
        HIDDEN = 4 * D
        ROPE_BASE = 10000.0
        EPS = 1e-06

        def rmsnorm(x, w):
            return x * jax.lax.rsqrt(jnp.mean(x * x, axis=-1, keepdims=True) + EPS) * w

        def safe_key_padding_mask(mask):
            all_pad = jnp.all(mask, axis=-1, keepdims=True)
            return jnp.where(all_pad, False, mask)

        def split_heads(x):
            b, t, _ = x.shape
            return x.reshape(b, t, H, HD).transpose(0, 2, 1, 3)

        def merge_heads(x):
            b, _, t, _ = x.shape
            return x.transpose(0, 2, 1, 3).reshape(b, t, H * HD)

        def apply_rope(x):
            t = x.shape[-2]
            pos = jnp.arange(t, dtype=jnp.float32)[:, None]
            freqs = jnp.exp(jnp.arange(0, HD, 2, dtype=jnp.float32) * (-math.log(ROPE_BASE) / HD))
            ang = pos * freqs[None, :]
            sin = jnp.sin(ang).astype(x.dtype)
            cos = jnp.cos(ang).astype(x.dtype)
            even, odd = (x[..., 0::2], x[..., 1::2])
            rot = jnp.stack((even * cos - odd * sin, even * sin + odd * cos), axis=-1)
            return rot.reshape(x.shape)

        def masked_attn(q, k, v, valid_keys):
            scores = jnp.einsum('bhqd,bhkd->bhqk', q, k) / math.sqrt(HD)
            scores = jnp.where(valid_keys[:, None, None, :], scores, jnp.finfo(scores.dtype).min)
            return jnp.einsum('bhqk,bhkd->bhqd', jax.nn.softmax(scores, axis=-1), v)
        x = rmsnorm(tokens, attn_norm_w)
        scale, shift = jnp.split(modulation @ film_w.T + film_b, 2, axis=-1)
        x = x * (1.0 + 0.1 * jnp.tanh(scale))[:, None, :] + shift[:, None, :]
        q, k, v = jnp.split(x @ qkv_w.T + qkv_b, 3, axis=-1)
        q, k, v = (split_heads(q), split_heads(k), split_heads(v))
        q, k = (apply_rope(q), apply_rope(k))
        valid = ~safe_key_padding_mask(padding_mask)
        tokens = tokens + merge_heads(masked_attn(q, k, v, valid)) @ out_w.T + out_b
        query = rmsnorm(tokens, sq_norm_w)
        src = rmsnorm(seq_tokens, s_norm_w)
        wq, wk, wv = jnp.split(mha_in_w, 3, axis=0)
        bq, bk, bv = jnp.split(mha_in_b, 3, axis=0)
        cq = split_heads(query @ wq.T + bq)
        ck = split_heads(src @ wk.T + bk)
        cv = split_heads(src @ wv.T + bv)
        svalid = ~safe_key_padding_mask(seq_mask)
        attended = merge_heads(masked_attn(cq, ck, cv, svalid)) @ mha_out_w.T + mha_out_b
        valid_rows = jnp.any(~seq_mask, axis=1).astype(attended.dtype)[:, None, None]
        update = attended * valid_rows
        gate = jax.nn.sigmoid(jnp.concatenate([tokens, update], axis=-1) @ gate_w.T + gate_b)
        tokens = tokens + gate * update
        h = rmsnorm(tokens, ffn_norm_w)
        g, val = jnp.split(h @ gu_w.T + gu_b, 2, axis=-1)
        return tokens + jax.nn.silu(g) * val @ down_w.T + down_b
    x = _L0_cond_ref(x, fside_BxSxS_0, cond_1024, L0_cond_attn_norm_w, L0_cond_qkv_w, L0_cond_qkv_b, L0_cond_out_w, L0_cond_out_b, L0_cond_film_w, L0_cond_film_b, L0_cond_sq_norm_w, L0_cond_s_norm_w, L0_cond_mha_in_w, L0_cond_mha_in_b, L0_cond_mha_out_w, L0_cond_mha_out_b, L0_cond_gate_w, L0_cond_gate_b, L0_cond_ffn_norm_w, L0_cond_gu_w, L0_cond_gu_b, L0_cond_down_w, L0_cond_down_b, mask_BxS_bk0, mask_BxS_bk0)
    return x

_drawn_inputs = setup_inputs


def setup_inputs(seed=0):
    import zlib

    import numpy as np

    out = dict(_drawn_inputs(seed))
    spreads = {'L0_cond_attn_norm_w': (1.0, 0.6),
     'L0_cond_qkv_b': (0.0, 0.358),
     'L0_cond_out_b': (0.0, 0.1),
     'L0_cond_film_b': (0.0, 0.8),
     'L0_cond_sq_norm_w': (1.0, 0.6),
     'L0_cond_s_norm_w': (1.0, 0.6),
     'L0_cond_mha_in_b': (0.0, 0.786),
     'L0_cond_mha_out_b': (0.0, 0.1),
     'L0_cond_gate_b': (0.0, 0.8),
     'L0_cond_ffn_norm_w': (1.0, 0.6),
     'L0_cond_gu_b': (0.0, 0.8),
     'L0_cond_down_b': (0.0, 0.1)}
    factors = {'fside_BxSxS_0': 8.0,
     'cond_1024': 5.229,
     'L0_cond_qkv_w': 4.299,
     'L0_cond_film_w': 4.972,
     'L0_cond_mha_in_w': 8.0,
     'L0_cond_mha_out_w': 4.862,
     'L0_cond_gate_w': 8.0,
     'L0_cond_gu_w': 3.762,
     'L0_cond_down_w': 3.687}
    for name, (base, spread) in spreads.items():
        noise = np.random.default_rng([zlib.crc32(name.encode()), seed]).standard_normal(out[name].shape)
        drawn = base * np.exp(spread * noise) if base else spread * noise
        out[name] = jnp.asarray(drawn.astype(out[name].dtype))
    for name, factor in factors.items():
        out[name] = (out[name] * factor).astype(out[name].dtype)
    return out
```

```python
import math
from contextlib import ExitStack

import concourse.bass as bass
from concourse import mybir

F32 = mybir.dt.float32
BF16 = mybir.dt.bfloat16
U8 = mybir.dt.uint8
ALU = mybir.AluOpType
ACT = mybir.ActivationFunctionType
AX = mybir.AxisListType

B, S, D = 32, 128, 128
H = 16
HD = D // H
HID = 4 * D
NG = 4
G = B // NG
T = NG * S
QH = 4
NQ = H // QH
EPS = 1e-6
SCALE = 1.0 / math.sqrt(HD)
MASKED = -1.0e38
PARTS = 3
R_MASK = PARTS * PARTS * HD
R_MAX = 96
R_END = R_MAX + PARTS
SELF, CROSS = 0, 1
MID, LATE = 1, 2

W_Q, W_K, W_V, W_OUT, W_FILM, W_CQ, W_CK, W_CV, W_MO, W_GATE, W_GU, W_DOWN = 0, 1, 2, 3, 4, 6, 7, 8, 9, 10, 12, 20
N_W = 24
P_Q, P_QX, P_K, P_KX, P_CQ, P_CK = range(6)
(C_ANW, C_SNW, C_SQW, C_FNW, C_OB, C_FB, C_MOB, C_GB, C_GUB, C_DB, C_QB, C_KB, C_CQB, C_CKB, C_QXB, C_KXB) = (
    0, 1, 2, 3, 4, 5, 7, 8, 9, 17, 18, 19, 20, 21, 22, 23)
N_C = 24
N_B_DMA = 4 + 10 + 2 * NG
N_W_DMA = 9


def wait(eng, sem, value):
    if not (isinstance(value, int) and value <= 0):
        eng.wait_ge(sem, value)


def build(nc, x, side, cond, mask, anw, qkv_w, qkv_b, out_w, out_b, film_w, film_b, sqw, snw, in_w, in_b,
          mo_w, mo_b, gate_w, gate_b, fnw, gu_w, gu_b, down_w, down_b, cos_t, sin_t, ident_t, out):
    with ExitStack() as ctx:
        def sb(name, shape, dt=F32):
            return ctx.enter_context(nc.sbuf_tensor(name, shape, dt))

        def sem(name):
            return ctx.enter_context(nc.semaphore(name))

        mask_dram = nc.dram_tensor("mask_rows", (B * S,), BF16, kind="Internal").ap()

        w_t = sb("w_t", [D, N_W, D])
        w_p = sb("w_p", [D, 6, D])
        bias_raw = sb("bias_raw", [C_QB, D])
        head_bias_raw = sb("head_bias_raw", [4, D])
        head_bias = sb("head_bias", [4, D])
        head_bias_x = sb("head_bias_x", [2, D])
        col = sb("col", [D, N_C])
        half_gate_b = sb("half_gate_b", [D, 1])
        half_g_b = sb("half_g_b", [D, 4])
        v_bias = [sb(f"v_bias{p}", [S, T]) for p in (SELF, CROSS)]
        cos = sb("cos", [D, S])
        sin = sb("sin", [D, S])
        ident = sb("ident", [128, 128])
        ident_b = sb("ident_b", [128, 128], BF16)
        mean_w = sb("mean_w", [D, 1])
        ones_pad = sb("ones_pad", [S, QH, 32])
        ones_row = sb("ones_row", [1, T], BF16)
        cond_sb = sb("cond_sb", [B, D])
        cond_t = sb("cond_t", [D, B])
        film_th = sb("film_th", [D, B])
        film_mul = sb("film_mul", [D, B])
        film_add = sb("film_add", [D, B])
        mask_u8 = sb("mask_u8", [B, S], U8)
        mask_f = sb("mask_f", [B, S])
        padded = sb("padded", [B, 1])
        some_valid = sb("some_valid", [B, 1])
        mask_rows = sb("mask_rows_sb", [B, S], BF16)
        valid_b = sb("valid_b", [B, 128])
        valid = sb("valid", [D, B])

        x_in = sb("x_in", [S, NG, D])
        s_in = sb("s_in", [S, NG, D])
        x_ss = sb("x_ss", [S, NG])
        s_ss = sb("s_ss", [S, NG])
        x_ms = sb("x_ms", [S, NG])
        s_ms = sb("s_ms", [S, NG])
        minus_half = sb("minus_half", [S, NG])
        ms2 = sb("ms2", [S, NG])
        r2 = sb("r2", [S, NG])
        x_r = sb("x_r", [S, NG])
        s_r = sb("s_r", [S, NG])
        x_n = sb("x_n", [S, NG, D])
        s_n = sb("s_n", [S, NG, D])
        x_t = sb("x_t", [D, T])
        xm_t = sb("xm_t", [D, T])
        s_t = sb("s_t", [D, T])
        rope_b = [sb(f"rope_b{n}", [D, T]) for n in range(2)]
        full = {n: sb(f"full_{n}", [D, T]) for n in ("q", "k", "ck")}
        rest = {n: sb(f"rest_{n}", [D, T]) for n in ("q", "k", "ck")}
        full["cq"], rest["cq"] = full["ck"], rest["ck"]
        part = {n: sb(f"part_{n}", [D, PARTS, T], BF16) for n in ("q", "k", "cq", "ck")}
        q_st = [sb(f"q_st{p}", [R_END, H, T], BF16) for p in (SELF, CROSS)]
        k_st = [sb(f"k_st{p}", [R_END, H, T], BF16) for p in (SELF, CROSS)]
        v_pad = [sb(f"v_pad{p}", [S, NG * NQ, 160]) for p in (SELF, CROSS)]
        top = sb("top", [S, NG, H])
        top_rest = sb("top_rest", [S, NG, H])
        top_part = sb("top_part", [S, NG, 128], BF16)
        top_t = sb("top_t", [PARTS * H, NG, S], BF16)
        probs = sb("probs", [S, 2, H * S])
        w_raw = probs[:, :, :].rearrange("s n x -> s (n x)")[:, 0:N_W * D].rearrange("o (n i) -> o n i", i=D)
        den = sb("den", [D, 2 * S])
        att = [sb(f"att{p}", [D, T]) for p in (SELF, CROSS)]
        t1 = sb("t1", [D, T])
        norm2 = sb("norm2", [D, T])
        upd = sb("upd", [D, T])
        gate_th = sb("gate_th", [D, T])
        r_wide = gate_th[:, :].rearrange("t (b d) -> t b d", b=NG)
        t2 = sb("t2", [D, T])
        norm3 = sb("norm3", [D, T])
        g_th = sb("g_th", [D, 2, T])
        g_u = sb("g_u", [D, 2, T])
        hid = sb("hid", [D, 4, T])
        y = sb("y", [S, NG, D])

        def bank(name):
            return ctx.enter_context(nc.psum_tensor(name, [128, 512], F32))

        ps_a = [bank("ps_a0"), bank("ps_a1")]
        ps_b = [bank("ps_b0"), bank("ps_b1")]
        ps_o = bank("ps_o")
        ps_d = [bank("ps_d0"), bank("ps_d1")]
        ps_m = bank("ps_m")
        ps_mb = ps_m[:, :].bitcast(BF16)

        w_loaded, b_loaded, c_loaded = sem("w_loaded"), sem("b_loaded"), sem("c_loaded")
        consts_set, eye_set = sem("consts_set"), sem("eye_set")
        bias_ordered = sem("bias_ordered")
        w_turned, w_kept, w_ordered = sem("w_turned"), sem("w_kept"), sem("w_ordered")
        cond_turned, cond_kept, film_made, film_tanh, film_set = (
            sem("cond_turned"), sem("cond_kept"), sem("film_made"), sem("film_tanh"), sem("film_set"))
        mask_step, mask_stored, valid_made = sem("mask_step"), sem("mask_stored"), sem("valid_made")
        rows_set = sem("rows_set")
        x_loaded, s_loaded = sem("x_loaded"), sem("s_loaded")
        x_squared, s_squared = sem("x_squared"), sem("s_squared")
        x_mean, s_mean, x_scaled, s_scaled = sem("x_mean"), sem("s_mean"), sem("x_scaled"), sem("s_scaled")
        x_normed, s_normed = sem("x_normed"), sem("s_normed")
        xm_turned, x_turned, s_turned, top_flipped, y_turned = (
            sem("xm_turned"), sem("x_turned"), sem("s_turned"), sem("top_flipped"), sem("y_turned"))
        xm_kept, x_kept, s_kept = sem("xm_kept"), sem("x_kept"), sem("s_kept")
        prod = {n: sem(f"{n}_product") for n in (
            "q", "qx", "k", "kx", "v", "ck", "cv", "mo", "gate", "ss3", "g", "val", "down", "out", "ss2", "cq")}
        roped = {n: sem(f"{n}_roped") for n in ("q", "k")}
        full_set = {n: sem(f"{n}_full") for n in ("q", "k", "cq", "ck")}
        hi_set = {n: sem(f"{n}_hi") for n in ("q", "k", "cq", "ck")}
        rest_set = {n: sem(f"{n}_rest") for n in ("q", "k", "cq", "ck")}
        mid_set = {n: sem(f"{n}_mid") for n in ("q", "k", "cq", "ck")}
        lo_set = {n: sem(f"{n}_lo") for n in ("q", "k", "cq", "ck")}
        stacked = {n: sem(f"{n}_stacked") for n in ("q", "k", "cq", "ck")}
        mask_in = [sem("self_mask_in"), sem("cross_mask_in")]
        v_kept = [sem("v_kept"), sem("cv_kept")]
        a_done, max_done, b_done, exp_done, pv_done = (
            sem("a_done"), sem("max_done"), sem("b_done"), sem("exp_done"), sem("pv_done"))
        top_hi, top_left, top_mid, top_split = sem("top_hi"), sem("top_left"), sem("top_mid"), sem("top_split")
        top_turned = sem("top_turned")
        top_in = [sem(f"top_in{b}") for b in range(NG)]
        den_inverted, att_set = sem("den_inverted"), sem("att_set")
        t1_set, sq2_set, query_set = sem("t1_set"), sem("sq2_set"), sem("query_set")
        mean2_set, root2_set, wide_set = sem("mean2_set"), sem("root2_set"), sem("wide_set")
        r2_turned, r3_turned = sem("r2_turned"), sem("r3_turned")
        upd_set, gate_tanh, gated_set, t2_set, sq3_set, h_set = (
            sem("upd_set"), sem("gate_tanh"), sem("gated_set"), sem("t2_set"), sem("sq3_set"), sem("h_set"))
        g_acted, silu_set, hid_set, y_set, y_kept, stored = (
            sem("g_acted"), sem("silu_set"), sem("hid_set"), sem("y_set"), sem("y_kept"), sem("stored"))

        def unit(g, ph, b):
            return g * 2 * NG + ph * NG + b

        def steps(window, loop):
            window(0, True, False)
            window(1, False, False)
            with loop(2, G - 1) as i:
                window(i, False, False)
            window(G - 1, False, True)

        block = ctx.enter_context(nc.Block())

        @block.sync
        def _(sp):
            sp.dma_start(ident[:, :], ident_t).then_inc(c_loaded, 16)
            sp.dma_start(cos[:, :], cos_t).then_inc(c_loaded, 16)
            sp.dma_start(sin[:, :], sin_t).then_inc(c_loaded, 16)
            sp.dma_start(cond_sb[:, :], cond).then_inc(c_loaded, 16)
            sp.dma_start(mask_u8[:, :], mask).then_inc(c_loaded, 16)

            def load_x(g):
                wait(sp, x_squared, g * NG)
                wait(sp, x_normed, g)
                wait(sp, x_kept, g)
                sp.dma_start(x_in[:, :, :], x[bass.ds(g * NG, NG), :, :].rearrange("b t d -> t b d")
                             ).then_inc(x_loaded, 16)

            def load_side(g):
                wait(sp, s_squared, g * NG)
                wait(sp, s_normed, g)
                sp.dma_start(s_in[:, :, :], side[bass.ds(g * NG, NG), :, :].rearrange("b t d -> t b d")
                             ).then_inc(s_loaded, 16)

            load_x(0)
            for at, src in ((W_Q, qkv_w.rearrange("(n o) i -> o n i", o=D)), (W_OUT, out_w.unsqueeze(1)),
                            (W_FILM, film_w.rearrange("(n o) i -> o n i", o=D)),
                            (W_CQ, in_w.rearrange("(n o) i -> o n i", o=D)), (W_MO, mo_w.unsqueeze(1)),
                            (W_GATE, gate_w.rearrange("o (n i) -> o n i", i=D)),
                            (W_GU, gu_w[0:HID, :].rearrange("(n o) i -> o n i", o=D)),
                            (W_GU + 4, gu_w[HID:2 * HID, :].rearrange("(n o) i -> o n i", o=D)),
                            (W_DOWN, down_w.rearrange("o (n i) -> o n i", i=D))):
                sp.dma_start(w_raw[:, at:at + src.shape[1], :], src).then_inc(w_loaded, 16)

            def bias_rows(tile, at, src):
                n = src.shape[0] // D
                sp.dma_start(tile[at:at + n, :], src.rearrange("(n p) -> n p", p=D)).then_inc(b_loaded, 16)

            for c, src in ((C_ANW, anw), (C_SNW, snw), (C_SQW, sqw), (C_FNW, fnw), (C_OB, out_b), (C_FB, film_b),
                           (C_MOB, mo_b), (C_GB, gate_b), (C_GUB, gu_b), (C_DB, down_b)):
                bias_rows(bias_raw, c, src)
            for c, src in enumerate((qkv_b[0:D], qkv_b[D:2 * D], in_b[0:D], in_b[D:2 * D])):
                bias_rows(head_bias_raw, c, src)
            for n in range(NG):
                for ph, src in ((SELF, qkv_b), (CROSS, in_b)):
                    sp.dma_start(v_bias[ph][:, n * D:(n + 1) * D],
                                 src[2 * D:3 * D].rearrange("(o n) -> o n", o=1).to_broadcast([S, D])
                                 ).then_inc(b_loaded, 16)
            load_side(0)
            sp.wait_ge(mask_step, 4)
            sp.dma_start(mask_dram.rearrange("(b s) -> b s", s=S), mask_rows[:, :]).then_inc(mask_stored, 16)
            sp.wait_ge(rows_set, 7)
            for tile in q_st:
                sp.dma_start(tile[R_MASK:R_MASK + 1, :, :],
                             ones_row[:, :].unsqueeze(1).to_broadcast([1, H, T])).then_inc(mask_stored, 16)
            sp.wait_ge(mask_stored, 48)

            def stack(n, p, g, ph):
                done = (hi_set, mid_set, lo_set)[p][n]
                sp.wait_ge(done, g + 1)
                tile = q_st[ph] if n in ("q", "cq") else k_st[ph]
                for o in range(PARTS):
                    row = HD * (PARTS * p + o) if n in ("q", "cq") else HD * (PARTS * o + p)
                    sp.dma_start(tile[row:row + HD, :, :], part[n][:, p, :]).then_inc(stacked[n], 16)

            def mask_row(g, ph):
                wait(sp, b_done, NQ * (unit(g, ph, 0) - NG))
                sp.dma_start(k_st[ph][R_MASK:R_MASK + 1, :, :],
                             mask_dram[bass.ds(g * T, T)].rearrange("(o s) -> o s", o=1).unsqueeze(1)
                             .to_broadcast([1, H, T])).then_inc(mask_in[ph], 16)

            def top_rows(g, ph, b):
                sp.wait_ge(top_turned, unit(g, ph, b) + 1)
                sp.dma_start(q_st[ph][R_MAX:R_END, :, b * S:(b + 1) * S], top_t[:, b, :]).then_inc(top_in[b], 16)

            def store(g):
                sp.wait_ge(y_kept, g + 1)
                sp.dma_start(out[bass.ds(g * NG, NG), :, :].rearrange("b t d -> t b d"), y[:, :, :]
                             ).then_inc(stored, 16)

            mask_row(0, SELF)
            for p in range(PARTS):
                stack("q", p, 0, SELF)
                stack("k", p, 0, SELF)

            def window(i, first, last):
                if not last:
                    load_x(i + 1)
                mask_row(i, CROSS)
                stack("ck", 0, i, CROSS)
                top_rows(i, SELF, 0)
                stack("ck", 1, i, CROSS)
                top_rows(i, SELF, 1)
                stack("ck", 2, i, CROSS)
                top_rows(i, SELF, 2)
                top_rows(i, SELF, 3)
                if not last:
                    load_side(i + 1)
                for p in range(PARTS):
                    stack("cq", p, i, CROSS)
                if not first:
                    store(i - 1)
                if last:
                    for b in range(NG):
                        top_rows(i, CROSS, b)
                    return
                mask_row(i + 1, SELF)
                top_rows(i, CROSS, 0)
                stack("q", 0, i + 1, SELF)
                top_rows(i, CROSS, 1)
                stack("q", 1, i + 1, SELF)
                stack("k", 0, i + 1, SELF)
                top_rows(i, CROSS, 2)
                stack("q", 2, i + 1, SELF)
                stack("k", 1, i + 1, SELF)
                top_rows(i, CROSS, 3)
                stack("k", 2, i + 1, SELF)

            steps(window, sp.Fori)
            store(G - 1)
            sp.wait_ge(stored, 16 * G)

        @block.gpsimd
        def _(pool):
            for tile in q_st + k_st:
                pool.memset(tile[64:R_MAX, :, :], 0.0).then_inc(rows_set, 1)
            pool.wait_ge(rows_set, 4)
            for tile in k_st:
                pool.memset(tile[R_MAX:R_END, :, :], 1.0).then_inc(rows_set, 1)
            pool.wait_ge(rows_set, 6)
            pool.memset(ones_row[:, :], 1.0).then_inc(rows_set, 1)
            pool.wait_ge(rows_set, 7)
            pool.wait_ge(consts_set, 3)

            def norm(g, raw, ms, mean, r, scaled, to, done):
                pool.wait_ge(mean, g + 1)
                pool.tensor_tensor(r[:, :], ms[:, :], minus_half[:, :], ALU.pow).then_inc(scaled, 1)
                pool.wait_ge(scaled, g + 1)
                pool.tensor_tensor(to[:, :, :], raw[:, :, :], r[:, :].unsqueeze(2).to_broadcast([S, NG, D]),
                                   ALU.mult).then_inc(done, 1)

            def norm_x(g):
                wait(pool, xm_kept, NG * g)
                norm(g, x_in, x_ms, x_mean, x_r, x_scaled, x_n, x_normed)

            def norm_side(g):
                wait(pool, s_kept, g)
                norm(g, s_in, s_ms, s_mean, s_r, s_scaled, s_n, s_normed)

            def rope_sum(n, g):
                s = "qk".index(n)
                pool.wait_ge(roped[n], 2 * g + 2)
                pool.tensor_tensor(full[n][:, :], full[n][:, :], rope_b[s][:, :], ALU.add
                                   ).then_inc(full_set[n], 1)

            def take_hi(n, g):
                pool.wait_ge(full_set[n], g + 1)
                pool.wait_ge(hi_set[n], g + 1)
                pool.tensor_tensor(rest[n][:, :], full[n][:, :], part[n][:, 0, :], ALU.subtract
                                   ).then_inc(rest_set[n], 1)

            def take_mid(n, g):
                pool.wait_ge(mid_set[n], g + 1)
                pool.tensor_tensor(part[n][:, 2, :], rest[n][:, :], part[n][:, 1, :], ALU.subtract
                                   ).then_inc(lo_set[n], 1)

            def qk(g):
                rope_sum("q", g)
                take_hi("q", g)
                rope_sum("k", g)
                take_mid("q", g)
                take_hi("k", g)
                take_mid("k", g)

            def root(g, which):
                pool.wait_ge(mean2_set, 2 * g + which)
                wait(pool, wide_set, 2 * g + which - 1)
                pool.tensor_tensor(r2[:, :], ms2[:, :], minus_half[:, :], ALU.pow).then_inc(root2_set, 1)

            norm_x(0)
            qk(0)
            norm_side(0)

            def window(i, first, last):
                take_hi("ck", i)
                take_mid("ck", i)
                if not first:
                    root(i - 1, LATE)
                if not last:
                    norm_x(i + 1)
                root(i, MID)
                take_hi("cq", i)
                take_mid("cq", i)
                if not last:
                    qk(i + 1)
                    norm_side(i + 1)

            steps(window, pool.Fori)
            root(G - 1, LATE)

        @block.scalar
        def _(act):
            def squares_x(g):
                act.wait_ge(x_loaded, 16 * (g + 1))
                wait(act, xm_kept, NG * g)
                wait(act, x_mean, g)
                for b in range(NG):
                    act.activation(x_n[:, b, :], x_in[:, b, :], ACT.Square, accum_out=x_ss[:, b:b + 1]
                                   ).then_inc(x_squared, 1)

            def squares_side(g):
                act.wait_ge(s_loaded, 16 * (g + 1))
                wait(act, s_kept, g)
                wait(act, s_mean, g)
                for b in range(NG):
                    act.activation(s_n[:, b, :], s_in[:, b, :], ACT.Square, accum_out=s_ss[:, b:b + 1]
                                   ).then_inc(s_squared, 1)

            def keep_xm(g):
                act.wait_ge(xm_turned, g + 1)
                wait(act, prod["v"], g)
                for b in range(NG):
                    act.activation(xm_t[:, b * S:(b + 1) * S], ps_m[:, b * S:(b + 1) * S], ACT.Identity,
                                   bias=film_add[:, bass.ds(g * NG + b, 1)],
                                   scale=film_mul[:, bass.ds(g * NG + b, 1)]).then_inc(xm_kept, 1)

            def keep_x(g):
                act.wait_ge(x_turned, g + 1)
                wait(act, t1_set, g)
                act.activation(x_t[:, :], ps_m[:, :], ACT.Copy).then_inc(x_kept, 1)

            def keep_side(g):
                act.wait_ge(s_turned, g + 1)
                wait(act, prod["cv"], g)
                act.activation(s_t[:, :], ps_m[:, :], ACT.Copy, scale=col[:, C_SNW:C_SNW + 1]).then_inc(s_kept, 1)

            def keep_full(n, g, bank_of, c, other, other_n):
                act.wait_ge(prod[n], g + 1)
                wait(act, rest_set[other], other_n)
                act.activation(full[n][:, :], bank_of[:, :], ACT.Identity, bias=col[:, c:c + 1]
                               ).then_inc(full_set[n], 1)

            def keep_hi(n, g):
                act.wait_ge(full_set[n], g + 1)
                wait(act, stacked[n], 16 * PARTS * PARTS * g)
                act.activation(part[n][:, 0, :], full[n][:, :], ACT.Copy).then_inc(hi_set[n], 1)

            def keep_mid(n, g):
                act.wait_ge(rest_set[n], g + 1)
                act.activation(part[n][:, 1, :], rest[n][:, :], ACT.Copy).then_inc(mid_set[n], 1)

            def keep_top(g, ph, b):
                act.wait_ge(top_flipped, unit(g, ph, b) + 1)
                wait(act, top_in[b], 16 * (2 * g + ph))
                act.activation(top_t[:, b, :], ps_mb[0:PARTS * H, 0:S], ACT.Copy).then_inc(top_turned, 1)

            def exps(g, ph, b, q):
                n = unit(g, ph, b)
                act.wait_ge(b_done, NQ * n + q + 1)
                if q == 0:
                    wait(act, pv_done, n - 1)
                act.activation(probs[:, b % 2, q * T:(q + 1) * T], ps_b[q % 2][:, :], ACT.Exp, scale=SCALE
                               ).then_inc(exp_done, 1)

            def gate(g):
                act.wait_ge(prod["gate"], g + 1)
                wait(act, t2_set, g)
                act.activation(gate_th[:, :], ps_d[1][:, :], ACT.Tanh, scale=0.5, bias=half_gate_b[:, :]
                               ).then_inc(gate_tanh, 1)

            def gated_unit(g, j):
                act.wait_ge(prod["g"], 4 * g + j + 1)
                wait(act, hid_set, 4 * g + max(j - 1, 0))
                act.activation(g_th[:, j % 2, :], ps_d[(j + 1) % 2][:, :], ACT.Tanh, scale=0.5,
                               bias=half_g_b[:, j:j + 1])
                act.activation(g_u[:, j % 2, :], ps_d[(j + 1) % 2][:, :], ACT.Identity, scale=0.5,
                               bias=half_g_b[:, j:j + 1]).then_inc(g_acted, 1)

            def keep_y(g):
                act.wait_ge(y_turned, g + 1)
                wait(act, stored, 16 * g)
                act.activation(y[:, :, :], ps_m[:, :].rearrange("t (b d) -> t b d", b=NG), ACT.Copy
                               ).then_inc(y_kept, 1)

            def square2(g):
                act.wait_ge(t1_set, g + 1)
                wait(act, prod["cq"], g)
                act.activation(norm2[:, :], t1[:, :], ACT.Square).then_inc(sq2_set, 1)

            def square3(g):
                act.wait_ge(t2_set, g + 1)
                wait(act, prod["val"], 4 * g)
                act.activation(norm3[:, :], t2[:, :], ACT.Square).then_inc(sq3_set, 1)

            squares_x(0)
            for n in (1, 3, 5):
                act.wait_ge(w_turned, n + 1)
                act.activation(w_t[:, 4 * n:4 * n + 4, :], (ps_a + ps_b + ps_d)[n][:, :].rearrange(
                    "i (n o) -> i n o", n=4), ACT.Copy).then_inc(w_kept, 1)
            act.wait_ge(cond_turned, 1)
            act.activation(cond_t[:, :], ps_m[:, 0:B], ACT.Copy).then_inc(cond_kept, 1)
            act.activation(col[:, :], ps_m[:, 128:128 + N_C], ACT.Copy).then_inc(cond_kept, 1)
            act.wait_ge(film_made, 1)
            act.wait_ge(cond_kept, 2)
            act.activation(film_th[:, :], ps_m[:, B:2 * B], ACT.Tanh, bias=col[:, C_FB:C_FB + 1]
                           ).then_inc(film_tanh, 1)
            act.wait_ge(film_set, 5)
            keep_xm(0)
            keep_x(0)
            keep_hi("q", 0)
            keep_mid("q", 0)
            keep_hi("k", 0)
            keep_mid("k", 0)
            squares_side(0)

            def attention_tail(g, ph, split=None):
                exps(g, ph, 0, 0)
                keep_top(g, ph, 1)
                for q in range(1, NQ):
                    exps(g, ph, 0, q)
                exps(g, ph, 1, 0)
                keep_top(g, ph, 2)
                for q in range(1, NQ):
                    exps(g, ph, 1, q)
                if split is not None:
                    keep_mid("k", split)
                exps(g, ph, 2, 0)
                keep_top(g, ph, 3)
                for q in range(1, NQ):
                    exps(g, ph, 2, q)
                for q in range(NQ):
                    exps(g, ph, 3, q)

            def window(i, first, last):
                keep_side(i)
                keep_full("ck", i, ps_d[0], C_CKB, "cq", i)
                keep_hi("ck", i)
                if not first:
                    gate(i - 1)
                keep_top(i, SELF, 0)
                if not first:
                    square3(i - 1)
                keep_mid("ck", i)
                attention_tail(i, SELF)
                if not last:
                    squares_x(i + 1)
                square2(i)
                if not first:
                    gated_unit(i - 1, 0)
                    gated_unit(i - 1, 1)
                    gated_unit(i - 1, 2)
                keep_full("cq", i, ps_a[0], C_CQB, "ck", i + 1)
                keep_hi("cq", i)
                keep_mid("cq", i)
                if not first:
                    gated_unit(i - 1, 3)
                    keep_y(i - 1)
                if not last:
                    keep_xm(i + 1)
                    keep_x(i + 1)
                keep_top(i, CROSS, 0)
                if not last:
                    keep_hi("q", i + 1)
                    keep_mid("q", i + 1)
                    keep_hi("k", i + 1)
                attention_tail(i, CROSS, None if last else i + 1)
                if not last:
                    squares_side(i + 1)

            steps(window, act.Fori)
            gate(G - 1)
            square3(G - 1)
            for j in range(4):
                gated_unit(G - 1, j)
            keep_y(G - 1)

        @block.tensor
        def _(pe):
            def turn(in_tile, g, ready, ready_n, done):
                pe.wait_ge(ready, ready_n)
                for b in range(NG):
                    mm = pe.transpose(ps_m[:, b * 128:(b + 1) * 128], in_tile(b), ident[:, :])
                mm.then_inc(done, 1)

            def dense(to, w, rhs, done, start=True, stop=True):
                mm = pe.matmul(to[:, :], w, rhs, start=start, stop=stop)
                if stop:
                    mm.then_inc(done, 1)

            def turn_xm(g):
                turn(lambda b: x_n[:, b, :], g, x_normed, g + 1, xm_turned)

            def turn_x(g):
                pe.wait_ge(xm_kept, NG * (g + 1))
                turn(lambda b: x_in[:, b, :], g, x_loaded, 16 * (g + 1), x_turned)

            def turn_side(g):
                turn(lambda b: s_n[:, b, :], g, s_normed, g + 1, s_turned)

            def q_product(g):
                pe.wait_ge(xm_kept, NG * (g + 1))
                dense(ps_d[0], w_p[:, P_Q, :], xm_t[:, :], prod["q"])

            def qx_product(g):
                dense(ps_d[1], w_p[:, P_QX, :], xm_t[:, :], prod["qx"])

            def k_product(g):
                pe.wait_ge(roped["q"], 2 * g + 1)
                dense(ps_d[0], w_p[:, P_K, :], xm_t[:, :], prod["k"])

            def kx_product(g):
                pe.wait_ge(roped["q"], 2 * g + 2)
                dense(ps_d[1], w_p[:, P_KX, :], xm_t[:, :], prod["kx"])

            def values(g, src, w, done):
                for b in range(NG):
                    mm = pe.matmul(ps_d[0][:, b * D:(b + 1) * D], src[:, b * S:(b + 1) * S], w,
                                   start=True, stop=True)
                mm.then_inc(done, 1)

            def v_product(g):
                pe.wait_ge(roped["k"], 2 * g + 1)
                values(g, xm_t, w_t[:, W_V, :], prod["v"])

            def ck_product(g):
                pe.wait_ge(s_kept, g + 1)
                pe.wait_ge(v_kept[SELF], g + 1)
                dense(ps_d[0], w_p[:, P_CK, :], s_t[:, :], prod["ck"])

            def cv_product(g):
                pe.wait_ge(full_set["ck"], g + 1)
                values(g, s_t, w_t[:, W_CV, :], prod["cv"])

            def max_scores(g, ph, b, q):
                n = unit(g, ph, b)
                name = ("q", "k") if ph == SELF else ("cq", "ck")
                if b == 0 and q == 0:
                    for one in name:
                        pe.wait_ge(stacked[one], 16 * PARTS * PARTS * (g + 1))
                    pe.wait_ge(mask_in[ph], 16 * (g + 1))
                wait(pe, max_done, NQ * n + q - 1)
                for j in range(QH):
                    h = QH * q + j
                    mm = pe.matmul(ps_a[q % 2][:, j * S:(j + 1) * S], q_st[ph][0:R_MAX, h, b * S:(b + 1) * S],
                                   k_st[ph][0:R_MAX, h, b * S:(b + 1) * S], start=True, stop=True)
                mm.then_inc(a_done, 1)

            def turn_top(g, ph, b):
                n = unit(g, ph, b)
                pe.wait_ge(top_split, n + 1)
                pe.transpose(ps_mb[:, 0:S], top_part[:, b, :], ident_b[:, :]).then_inc(top_flipped, 1)

            def prob_scores(g, ph, b, q):
                n = unit(g, ph, b)
                if q == 0:
                    pe.wait_ge(top_in[b], 16 * (2 * g + ph + 1))
                wait(pe, exp_done, NQ * n + q - 1)
                for j in range(QH):
                    h = QH * q + j
                    mm = pe.matmul(ps_b[q % 2][:, j * S:(j + 1) * S], k_st[ph][0:R_END, h, b * S:(b + 1) * S],
                                   q_st[ph][0:R_END, h, b * S:(b + 1) * S], start=True, stop=True)
                mm.then_inc(b_done, 1)

            def weigh(g, ph, b, q):
                n = unit(g, ph, b)
                if q == 0:
                    pe.wait_ge(exp_done, NQ * (n + 1))
                    pe.wait_ge(v_kept[ph], g + 1)
                    if b % 2 == 0:
                        wait(pe, att_set, g * NG + ph * 2 + b // 2)
                at = (b % 2) * S + (2 * S if q >= 2 else 0)
                for j in ((0, 1), (2, 3))[q % 2]:
                    for c in range(NQ):
                        w = (v_pad[ph][:, b * NQ + c, j * 32:(j + 1) * 32] if q < 2 else ones_pad[:, j, :])
                        mm = pe.matmul(ps_o[32 * c:32 * c + 32, at:at + S], w,
                                       probs[:, b % 2, (QH * c + j) * S:(QH * c + j + 1) * S],
                                       start=(j == 0), stop=(j == QH - 1))
                if q == 3:
                    mm.then_inc(pv_done, 1)

            def mo_product(g):
                pe.wait_ge(att_set, NG * (g + 1))
                dense(ps_d[1], w_t[:, W_MO, :], att[CROSS][:, :], prod["mo"])

            def gate_product(g):
                pe.wait_ge(upd_set, g + 1)
                dense(ps_d[1], w_t[:, W_GATE, :], t1[:, :], None, stop=False)
                dense(ps_d[1], w_t[:, W_GATE + 1, :], upd[:, :], prod["gate"], start=False)

            def token_means(g, squares, squares_set, bank_of, done):
                pe.wait_ge(squares_set, g + 1)
                for b in range(NG):
                    mm = pe.matmul(bank_of[:, b:b + 1], squares[:, b * S:(b + 1) * S], mean_w[:, :],
                                   start=True, stop=True)
                mm.then_inc(done, 1)

            def turn_factors(g, which, bank_of, done):
                pe.wait_ge(wide_set, 2 * g + which)
                for b in range(NG):
                    mm = pe.transpose(bank_of[:, b * S:(b + 1) * S], r_wide[:, b, :], ident[:, :])
                mm.then_inc(done, 1)

            def ss3_product(g):
                token_means(g, norm3, sq3_set, ps_d[0], prod["ss3"])

            def out_product(g):
                pe.wait_ge(att_set, NG * g + 2)
                pe.wait_ge(max_done, NQ * unit(g, CROSS, 0))
                dense(ps_a[0], w_t[:, W_OUT, :], att[SELF][:, :], prod["out"])

            def ss2_product(g):
                token_means(g, norm2, sq2_set, ps_a[1], prod["ss2"])

            def cq_product(g):
                pe.wait_ge(query_set, g + 1)
                dense(ps_a[0], w_p[:, P_CQ, :], norm2[:, :], prod["cq"])

            def mlp_up(g, j):
                if j == 0:
                    pe.wait_ge(h_set, g + 1)
                    pe.wait_ge(gate_tanh, g + 1)
                if j >= 2:
                    pe.wait_ge(g_acted, 4 * g + j - 1)
                dense(ps_d[(j + 1) % 2], w_t[:, W_GU + j, :], norm3[:, :], prod["g"])
                if j >= 2:
                    pe.wait_ge(hid_set, 4 * g + j - 1)
                dense(ps_b[j % 2], w_t[:, W_GU + 4 + j, :], norm3[:, :], prod["val"])

            def mlp_down(g):
                pe.wait_ge(g_acted, 4 * g + 3)
                for j in range(4):
                    pe.wait_ge(hid_set, 4 * g + j + 1)
                    dense(ps_d[1], w_t[:, W_DOWN + j, :], hid[:, j, :], prod["down"], start=(j == 0), stop=(j == 3))

            def turn_y(g):
                turn(lambda b: t2[:, b * S:(b + 1) * S], g, y_set, g + 1, y_turned)

            pe.wait_ge(w_loaded, 16 * N_W_DMA)
            pe.wait_ge(c_loaded, 16 * 5)
            for n in range(6):
                for m in range(4):
                    mm = pe.transpose((ps_a + ps_b + ps_d)[n][:, m * D:(m + 1) * D], w_raw[:, 4 * n + m, :],
                                      ident[:, :])
                mm.then_inc(w_turned, 1)
            pe.wait_ge(b_loaded, 16 * N_B_DMA)
            pe.wait_ge(bias_ordered, 3)
            pe.transpose(ps_m[:, 0:B], cond_sb[:, :], ident[0:B, 0:B])
            for at, rows in ((C_ANW, bias_raw), (C_QB, head_bias), (C_QXB, head_bias_x)):
                n = rows.shape[0]
                mm = pe.transpose(ps_m[:, 128 + at:128 + at + n], rows[:, :], ident[0:n, 0:n])
            mm.then_inc(cond_turned, 1)
            pe.wait_ge(cond_kept, 2)
            pe.wait_ge(w_kept, 6)
            pe.wait_ge(mask_step, 5)
            pe.matmul(ps_m[:, B:2 * B], w_t[:, W_FILM, :], cond_t[:, :], start=True, stop=True)
            pe.matmul(ps_m[:, 2 * B:3 * B], w_t[:, W_FILM + 1, :], cond_t[:, :], start=True, stop=True)
            pe.matmul(ps_m[:, 3 * B:4 * B], valid_b[:, :], ident[0:B, 0:B], start=True, stop=True
                      ).then_inc(film_made, 1)
            pe.wait_ge(film_set, 5)
            pe.wait_ge(consts_set, 3 + QH)
            pe.wait_ge(w_ordered, 8)
            pe.wait_ge(eye_set, 2)
            turn_xm(0)
            turn_x(0)
            q_product(0)
            qx_product(0)
            k_product(0)
            kx_product(0)
            v_product(0)

            def attention_tail(g, ph, late=None):
                for q in range(NQ):
                    max_scores(g, ph, 2, q)
                    prob_scores(g, ph, 0, q)
                    if q == 1:
                        pe.wait_ge(top_turned, unit(g, ph, 1))
                        turn_top(g, ph, 1)
                if late is not None:
                    turn_factors(late, LATE, ps_d[0], r3_turned)
                for q in range(NQ):
                    max_scores(g, ph, 3, q)
                    weigh(g, ph, 0, q)
                    prob_scores(g, ph, 1, q)
                    if q == 1:
                        pe.wait_ge(top_turned, unit(g, ph, 2))
                        turn_top(g, ph, 2)
                for q in range(NQ):
                    weigh(g, ph, 1, q)
                    prob_scores(g, ph, 2, q)
                    if q == 1:
                        pe.wait_ge(top_turned, unit(g, ph, 3))
                        turn_top(g, ph, 3)
                for q in range(NQ):
                    weigh(g, ph, 2, q)
                    prob_scores(g, ph, 3, q)
                for q in range(NQ):
                    weigh(g, ph, 3, q)

            def window(i, first, last):
                max_scores(i, SELF, 0, 0)
                if first:
                    pe.wait_ge(x_kept, 1)
                else:
                    pe.wait_ge(top_turned, unit(i, SELF, 0))
                turn_side(i)
                max_scores(i, SELF, 0, 1)
                ck_product(i)
                max_scores(i, SELF, 0, 2)
                if not first:
                    pe.wait_ge(roped["k"], 2 * i + 2)
                    mo_product(i - 1)
                max_scores(i, SELF, 0, 3)
                cv_product(i)
                max_scores(i, SELF, 1, 0)
                if not first:
                    gate_product(i - 1)
                max_scores(i, SELF, 1, 1)
                pe.wait_ge(s_kept, i + 1)
                turn_top(i, SELF, 0)
                max_scores(i, SELF, 1, 2)
                if not first:
                    pe.wait_ge(v_kept[CROSS], i + 1)
                    ss3_product(i - 1)
                max_scores(i, SELF, 1, 3)
                attention_tail(i, SELF, None if first else i - 1)
                out_product(i)
                if not first:
                    mlp_up(i - 1, 0)
                ss2_product(i)
                if not first:
                    mlp_up(i - 1, 1)
                turn_factors(i, MID, ps_a[1], r2_turned)
                if not first:
                    mlp_up(i - 1, 2)
                cq_product(i)
                if not first:
                    mlp_up(i - 1, 3)
                    mlp_down(i - 1)
                    pe.wait_ge(top_turned, unit(i, CROSS, 0))
                    turn_y(i - 1)
                max_scores(i, CROSS, 0, 0)
                if not last:
                    if first:
                        pe.wait_ge(top_turned, unit(i, CROSS, 0))
                    else:
                        pe.wait_ge(y_kept, i)
                    turn_xm(i + 1)
                max_scores(i, CROSS, 0, 1)
                if not last:
                    turn_x(i + 1)
                max_scores(i, CROSS, 0, 2)
                if not last:
                    if first:
                        pe.wait_ge(v_kept[CROSS], 1)
                    else:
                        pe.wait_ge(g_acted, 4 * i)
                    q_product(i + 1)
                max_scores(i, CROSS, 0, 3)
                if not last:
                    if first:
                        pe.wait_ge(roped["k"], 2)
                    else:
                        pe.wait_ge(y_set, i)
                    qx_product(i + 1)
                max_scores(i, CROSS, 1, 0)
                if not last:
                    k_product(i + 1)
                max_scores(i, CROSS, 1, 1)
                if last:
                    pe.wait_ge(y_kept, i)
                else:
                    pe.wait_ge(x_kept, i + 2)
                turn_top(i, CROSS, 0)
                max_scores(i, CROSS, 1, 2)
                if not last:
                    kx_product(i + 1)
                max_scores(i, CROSS, 1, 3)
                if not last:
                    v_product(i + 1)
                attention_tail(i, CROSS)

            steps(window, pe.Fori)
            pe.wait_ge(y_set, G - 1)
            mo_product(G - 1)
            gate_product(G - 1)
            pe.wait_ge(g_acted, 4 * (G - 1))
            ss3_product(G - 1)
            turn_factors(G - 1, LATE, ps_d[0], r3_turned)
            for j in range(4):
                mlp_up(G - 1, j)
            mlp_down(G - 1)
            pe.wait_ge(top_turned, unit(G, SELF, 0))
            turn_y(G - 1)

        @block.vector
        def _(dve):
            def means_x(g):
                dve.wait_ge(x_squared, NG * (g + 1))
                wait(dve, x_scaled, g)
                dve.tensor_scalar(x_ms[:, :], x_ss[:, :], 1.0 / D, EPS, ALU.mult, ALU.add).then_inc(x_mean, 1)

            def means_side(g):
                dve.wait_ge(s_squared, NG * (g + 1))
                wait(dve, s_scaled, g)
                dve.tensor_scalar(s_ms[:, :], s_ss[:, :], 1.0 / D, EPS, ALU.mult, ALU.add).then_inc(s_mean, 1)

            def by_batch(ap):
                return ap.rearrange("p (b t) -> p b t", b=NG)

            def rope(n, g, swapped):
                s = "qk".index(n)
                c = {"q": (C_QB, C_QXB), "k": (C_KB, C_KXB)}[n][swapped]
                src = ps_d[swapped]
                dve.wait_ge(prod[n + ("x" if swapped else "")], g + 1)
                wait(dve, rest_set[n], g)
                table = (cos, sin)[swapped][:, :].unsqueeze(1).to_broadcast([D, NG, S])
                dve.scalar_tensor_tensor(by_batch((rope_b[s] if swapped else full[n])[:, :]), by_batch(src[:, :]),
                                         col[:, c:c + 1], table, ALU.add, ALU.mult).then_inc(roped[n], 1)

            def keep_v(g, ph):
                dve.wait_ge(prod[("v", "cv")[ph]], g + 1)
                wait(dve, pv_done, unit(g, ph, 0) - NG)
                to = v_pad[ph][:, :, :].rearrange("t n (j c) -> t n j c", j=QH)[:, :, :, 0:HD]
                dve.tensor_tensor(to, ps_d[0][:, :].rearrange("t (n j d) -> t n j d", j=QH, d=HD),
                                  v_bias[ph][:, :].rearrange("t (n j d) -> t n j d", j=QH, d=HD), ALU.add
                                  ).then_inc(v_kept[ph], 1)

            def maxima(g, ph, b, q):
                n = unit(g, ph, b)
                dve.wait_ge(a_done, NQ * n + q + 1)
                dve.tensor_reduce(top[:, b, QH * q:QH * (q + 1)], ps_a[q % 2][:, :].rearrange(
                    "p (h k) -> p h k", h=QH), AX.X, ALU.max).then_inc(max_done, 1)

            def split_top(g, ph, b):
                n = unit(g, ph, b)
                parts = [top_part[:, b, p * H:(p + 1) * H] for p in range(PARTS)]
                dve.wait_ge(max_done, NQ * (n + 1))
                wait(dve, top_flipped, n - NG + 1)
                dve.tensor_scalar(parts[0], top[:, b, :], -1.0, None, ALU.mult).then_inc(top_hi, 1)
                dve.wait_ge(top_hi, n + 1)
                dve.scalar_tensor_tensor(top_rest[:, b, :], top[:, b, :], -1.0, parts[0], ALU.mult, ALU.subtract
                                         ).then_inc(top_left, 1)
                dve.wait_ge(top_left, n + 1)
                dve.tensor_copy(parts[1], top_rest[:, b, :]).then_inc(top_mid, 1)
                dve.wait_ge(top_mid, n + 1)
                dve.tensor_tensor(parts[2], top_rest[:, b, :], parts[1], ALU.subtract).then_inc(top_split, 1)

            def attended(g, ph, pair):
                n = g * NG + ph * 2 + pair
                dve.wait_ge(pv_done, 2 * n + 2)
                dve.reciprocal(den[:, :], ps_o[:, 2 * S:4 * S]).then_inc(den_inverted, 1)
                dve.wait_ge(den_inverted, n + 1)
                wait(dve, prod[("out", "mo")[ph]], g)
                dve.tensor_tensor(att[ph][:, pair * 2 * S:(pair + 1) * 2 * S], ps_o[:, 0:2 * S], den[:, :],
                                  ALU.mult).then_inc(att_set, 1)

            def residual1(g):
                dve.wait_ge(prod["out"], g + 1)
                dve.wait_ge(x_kept, g + 1)
                wait(dve, prod["gate"], g)
                dve.scalar_tensor_tensor(t1[:, :], ps_a[0][:, :], col[:, C_OB:C_OB + 1], x_t[:, :], ALU.add, ALU.add
                                         ).then_inc(t1_set, 1)

            def mean_of(g, which, bank_of, made):
                dve.wait_ge(made, g + 1)
                dve.tensor_scalar(ms2[:, :], bank_of[:, 0:NG], EPS, None, ALU.add).then_inc(mean2_set, 1)

            def widen(g, which):
                dve.wait_ge(root2_set, 2 * g + which)
                dve.tensor_copy(r_wide[:, :, :], r2[:, :].unsqueeze(2).to_broadcast([S, NG, D])
                                ).then_inc(wide_set, 1)

            def normed(g, t, c, bank_of, turned, to, done):
                dve.wait_ge(turned, g + 1)
                dve.scalar_tensor_tensor(to[:, :], t[:, :], col[:, c:c + 1], bank_of[:, :], ALU.mult, ALU.mult
                                         ).then_inc(done, 1)

            def update(g):
                dve.wait_ge(prod["mo"], g + 1)
                wait(dve, prod["gate"], g)
                keep = valid[:, bass.ds(g * NG, NG)].unsqueeze(2).to_broadcast([D, NG, S])
                dve.scalar_tensor_tensor(by_batch(upd[:, :]), by_batch(ps_d[1][:, :]), col[:, C_MOB:C_MOB + 1],
                                         keep, ALU.add, ALU.mult).then_inc(upd_set, 1)

            def residual2(g):
                dve.wait_ge(gate_tanh, g + 1)
                dve.scalar_tensor_tensor(gate_th[:, :], gate_th[:, :], 1.0, upd[:, :], ALU.add, ALU.mult
                                         ).then_inc(gated_set, 1)
                dve.wait_ge(gated_set, g + 1)
                wait(dve, y_kept, g)
                dve.scalar_tensor_tensor(t2[:, :], gate_th[:, :], 0.5, t1[:, :], ALU.mult, ALU.add
                                         ).then_inc(t2_set, 1)

            def silu_of(g, j):
                dve.wait_ge(g_acted, 4 * g + j + 1)
                dve.scalar_tensor_tensor(g_th[:, j % 2, :], g_th[:, j % 2, :], 1.0, g_u[:, j % 2, :], ALU.add, ALU.mult
                                         ).then_inc(silu_set, 1)

            def hidden(g, j):
                dve.wait_ge(silu_set, 4 * g + j + 1)
                dve.wait_ge(prod["val"], 4 * g + j + 1)
                wait(dve, prod["down"], g)
                dve.scalar_tensor_tensor(hid[:, j, :], ps_b[j % 2][:, :], col[:, C_GUB + 4 + j:C_GUB + 5 + j],
                                         g_th[:, j % 2, :], ALU.add, ALU.mult).then_inc(hid_set, 1)

            def residual3(g):
                dve.wait_ge(prod["down"], g + 1)
                dve.scalar_tensor_tensor(t2[:, :], ps_d[1][:, :], col[:, C_DB:C_DB + 1], t2[:, :], ALU.add, ALU.add
                                         ).then_inc(y_set, 1)

            dve.memset(ones_pad[:, :, :], 0.0).then_inc(consts_set, 1)
            dve.memset(mean_w[:, :], 1.0 / D).then_inc(consts_set, 1)
            dve.memset(minus_half[:, :], -0.5).then_inc(consts_set, 1)
            dve.wait_ge(consts_set, 3)
            for j in range(QH):
                dve.memset(ones_pad[:, j, j * HD:(j + 1) * HD], 1.0).then_inc(consts_set, 1)
            for tile in v_pad:
                dve.memset(tile[:, :, :], 0.0).then_inc(consts_set, 1)
            dve.wait_ge(c_loaded, 16 * 5)
            dve.tensor_copy(ident_b[:, :], ident[:, :]).then_inc(eye_set, 1)
            dve.memset(top_part[:, :, :], 0.0).then_inc(eye_set, 1)
            dve.wait_ge(eye_set, 2)
            dve.tensor_copy(mask_f[:, :], mask_u8[:, :]).then_inc(mask_step, 1)
            dve.wait_ge(mask_step, 1)
            dve.tensor_reduce(padded[:, :], mask_f[:, :], AX.X, ALU.min).then_inc(mask_step, 1)
            dve.wait_ge(mask_step, 2)
            dve.tensor_scalar(some_valid[:, :], padded[:, :], -1.0, 1.0, ALU.mult, ALU.add).then_inc(mask_step, 1)
            dve.wait_ge(mask_step, 3)
            dve.tensor_scalar(mask_rows[:, :], mask_f[:, :], some_valid[:, :], MASKED, ALU.mult, ALU.mult
                              ).then_inc(mask_step, 1)
            dve.tensor_scalar(valid_b[:, :], mask_f[:, :], 0.0, some_valid[:, :], ALU.mult, ALU.add
                              ).then_inc(mask_step, 1)
            dve.wait_ge(b_loaded, 16 * N_B_DMA)
            dve.tensor_copy(head_bias[:, :].rearrange("r (d h) -> r d h", d=HD),
                            head_bias_raw[:, :].rearrange("r (h d) -> r d h", d=HD)).then_inc(bias_ordered, 1)
            for two in range(2):
                dve.tensor_copy(
                    head_bias_x[:, :].rearrange("r (m two h) -> r two m h", two=2, h=H)[:, two, :, :],
                    head_bias_raw[0:2, :].rearrange("r (h m two) -> r two m h", two=2, h=H)[:, 1 - two, :, :]
                ).then_inc(bias_ordered, 1)
            means_x(0)
            for n in (0, 2, 4):
                dve.wait_ge(w_turned, n + 1)
                dve.tensor_copy(w_t[:, 4 * n:4 * n + 4, :], (ps_a + ps_b + ps_d)[n][:, :].rearrange(
                    "i (n o) -> i n o", n=4)).then_inc(w_kept, 1)
            dve.wait_ge(w_kept, 6)
            for p, w in ((P_Q, W_Q), (P_K, W_K), (P_CQ, W_CQ), (P_CK, W_CK)):
                dve.tensor_copy(w_p[:, p, :].rearrange("i (d h) -> i d h", d=HD),
                                w_t[:, w, :].rearrange("i (h d) -> i d h", d=HD)).then_inc(w_ordered, 1)
            for p, w in ((P_QX, W_Q), (P_KX, W_K)):
                for two in range(2):
                    dve.tensor_copy(
                        w_p[:, p, :].rearrange("i (m two h) -> i two m h", two=2, h=H)[:, two, :, :],
                        w_t[:, w, :].rearrange("i (h m two) -> i two m h", two=2, h=H)[:, 1 - two, :, :]
                    ).then_inc(w_ordered, 1)
            dve.wait_ge(cond_kept, 2)
            dve.tensor_scalar(half_gate_b[:, :], col[:, C_GB:C_GB + 1], 0.5, None, ALU.mult)
            dve.tensor_scalar(half_g_b[:, :], col[:, C_GUB:C_GUB + 4], 0.5, None, ALU.mult).then_inc(film_set, 1)
            dve.wait_ge(film_tanh, 1)
            dve.tensor_scalar(film_th[:, :], film_th[:, :], 0.1, 1.0, ALU.mult, ALU.add).then_inc(film_set, 1)
            dve.wait_ge(film_set, 2)
            dve.tensor_scalar(film_mul[:, :], film_th[:, :], col[:, C_ANW:C_ANW + 1], None, ALU.mult
                              ).then_inc(film_set, 1)
            dve.tensor_scalar(film_add[:, :], ps_m[:, 2 * B:3 * B], col[:, C_FB + 1:C_FB + 2], None, ALU.add
                              ).then_inc(film_set, 1)
            dve.tensor_copy(valid[:, :], ps_m[:, 3 * B:4 * B]).then_inc(film_set, 1)
            rope("q", 0, 0)
            rope("q", 0, 1)
            rope("k", 0, 0)
            rope("k", 0, 1)
            dve.wait_ge(consts_set, 5 + QH)
            keep_v(0, SELF)
            means_side(0)

            def attention_tail(g, ph, late=None):
                for q in range(NQ):
                    maxima(g, ph, 2, q)
                split_top(g, ph, 2)
                if late is not None:
                    widen(late, LATE)
                for q in range(NQ):
                    maxima(g, ph, 3, q)
                split_top(g, ph, 3)
                if late is not None:
                    normed(late, t2, C_FNW, ps_d[0], r3_turned, norm3, h_set)
                attended(g, ph, 0)

            def window(i, first, last):
                for q in range(NQ):
                    maxima(i, SELF, 0, q)
                split_top(i, SELF, 0)
                if not first:
                    update(i - 1)
                maxima(i, SELF, 1, 0)
                keep_v(i, CROSS)
                maxima(i, SELF, 1, 1)
                if not first:
                    residual2(i - 1)
                maxima(i, SELF, 1, 2)
                maxima(i, SELF, 1, 3)
                split_top(i, SELF, 1)
                if not first:
                    mean_of(i - 1, LATE, ps_d[0], prod["ss3"])
                attention_tail(i, SELF, None if first else i - 1)
                if not last:
                    means_x(i + 1)
                attended(i, SELF, 1)
                residual1(i)
                mean_of(i, MID, ps_a[1], prod["ss2"])
                if not first:
                    silu_of(i - 1, 0)
                    hidden(i - 1, 0)
                widen(i, MID)
                normed(i, t1, C_SQW, ps_a[1], r2_turned, norm2, query_set)
                if not first:
                    for j in (1, 2, 3):
                        silu_of(i - 1, j)
                        hidden(i - 1, j)
                    residual3(i - 1)
                for q in range(3):
                    maxima(i, CROSS, 0, q)
                if not last:
                    rope("q", i + 1, 0)
                maxima(i, CROSS, 0, 3)
                split_top(i, CROSS, 0)
                if not last:
                    rope("q", i + 1, 1)
                maxima(i, CROSS, 1, 0)
                if not last:
                    rope("k", i + 1, 0)
                maxima(i, CROSS, 1, 1)
                maxima(i, CROSS, 1, 2)
                if not last:
                    rope("k", i + 1, 1)
                maxima(i, CROSS, 1, 3)
                split_top(i, CROSS, 1)
                if not last:
                    keep_v(i + 1, SELF)
                attention_tail(i, CROSS)
                if not last:
                    means_side(i + 1)
                attended(i, CROSS, 1)

            steps(window, dve.Fori)
            update(G - 1)
            residual2(G - 1)
            mean_of(G - 1, LATE, ps_d[0], prod["ss3"])
            widen(G - 1, LATE)
            normed(G - 1, t2, C_FNW, ps_d[0], r3_turned, norm3, h_set)
            for j in range(4):
                silu_of(G - 1, j)
                hidden(G - 1, j)
            residual3(G - 1)


_INS = ['x', 'fside_BxSxS_0', 'cond_1024', 'mask_BxS_bk0', 'L0_cond_attn_norm_w', 'L0_cond_qkv_w',
        'L0_cond_qkv_b', 'L0_cond_out_w', 'L0_cond_out_b', 'L0_cond_film_w', 'L0_cond_film_b',
        'L0_cond_sq_norm_w', 'L0_cond_s_norm_w', 'L0_cond_mha_in_w', 'L0_cond_mha_in_b', 'L0_cond_mha_out_w',
        'L0_cond_mha_out_b', 'L0_cond_gate_w', 'L0_cond_gate_b', 'L0_cond_ffn_norm_w', 'L0_cond_gu_w',
        'L0_cond_gu_b', 'L0_cond_down_w', 'L0_cond_down_b']


def rope_tables():
    import numpy as np
    freqs = np.exp(np.arange(0, HD, 2, dtype=np.float32) * np.float32(-math.log(10000.0) / HD))
    angles = np.arange(S, dtype=np.float32)[None, :] * freqs[:, None]
    sign = np.array([-1.0, 1.0], np.float32)
    cos_rows = np.repeat(np.cos(angles), 2, axis=0)
    sin_rows = np.repeat(np.sin(angles), 2, axis=0) * np.tile(sign, HD // 2)[:, None]
    return (np.ascontiguousarray(np.repeat(cos_rows, H, axis=0), np.float32),
            np.ascontiguousarray(np.repeat(sin_rows, H, axis=0), np.float32))


def kernel(**inputs):
    import numpy as np
    import concourse.bacc as bacc
    from concourse.bass_utils import run_bass_kernel_spmd

    nc = bacc.Bacc("TRN2", target_bir_lowering=False, num_devices=1)
    arrays, args = {}, []

    def given(name, a):
        arrays[name] = a
        args.append(nc.dram_tensor(name, a.shape, mybir.dt.from_np(a.dtype), kind="ExternalInput").ap())

    for name in _INS:
        a = np.ascontiguousarray(inputs[name])
        given(f"in_{name}", a)
    cos_table, sin_table = rope_tables()
    given("cos_table", cos_table)
    given("sin_table", sin_table)
    given("identity", np.eye(128, dtype=np.float32))
    args.append(nc.dram_tensor("out", (B, S, D), F32, kind="ExternalOutput").ap())
    build(nc, *args)
    r = run_bass_kernel_spmd(nc, [arrays], core_ids=[0])
    return r.results[0]["out"]
```
